# Optimizing a Trainium2 kernel written in Bass

```python
import numpy as np
import jax
import jax.numpy as jnp

def _softmax(x, axis=-1):
    return jax.nn.softmax(x, axis=axis)

def _gelu(x):
    return jax.nn.gelu(x, approximate=True)

def _silu(x):
    return jax.nn.silu(x)

def _sigmoid(x):
    return jax.nn.sigmoid(x)

def _layernorm(x, axis=-1, eps=1e-05):
    m = jnp.mean(x, axis=axis, keepdims=True)
    v = jnp.var(x, axis=axis, keepdims=True)
    return (x - m) / jnp.sqrt(v + eps)

def _scatter_add(tgt, idx, src, axis=0):
    return tgt.at[idx].add(src)

def _segment_sum(src, seg, n):
    return jax.ops.segment_sum(src, seg, n)
kernel_name = 'mk_gnn_preln_d1_gnn_r8_57709c'

def setup_inputs(seed: int=0):
    np.random.seed(seed)
    _w = jnp.asarray

    def _rec_inputs():
        import jax
        import jax.numpy as jnp
        _gk = jax.random.key(seed)
        x = -0.0003713 + 1 * jax.random.normal(jax.random.fold_in(_gk, 1), (12500, 128), jnp.float32)
        src = jax.random.randint(jax.random.fold_in(_gk, 2), (200000,), 0, 12500, jnp.int32)
        dst = jax.random.randint(jax.random.fold_in(_gk, 3), (200000,), 0, 12500, jnp.int32)
        _o = jnp.argsort(dst, stable=True)
        src = src[_o]
        dst = dst[_o]
        return (x, src, dst)
    x, src, dst = _rec_inputs()

    def _L0_gnn_setup():
        import jax, jax.numpy as jnp
        import numpy as np
        N, E, D, H = (12500, 75000, 128, 512)
        key = jax.random.key(seed)
        ks = jax.random.split(key, 9)
        s = 0.05
        return {'z': jax.random.normal(ks[0], (N, D), dtype=jnp.float32), 'edge_index': jax.random.randint(ks[1], (2, E), 0, N, dtype=jnp.int64), 'Wg': jax.random.normal(ks[2], (D, D), dtype=jnp.float32) * s, 'Ws': jax.random.normal(ks[3], (D, D), dtype=jnp.float32) * s, 'bg': jnp.zeros((D,), dtype=jnp.float32), 'W1': jax.random.normal(ks[4], (D, H), dtype=jnp.float32) * s, 'b1': jnp.zeros((H,), dtype=jnp.float32), 'W2': jax.random.normal(ks[5], (H, H), dtype=jnp.float32) * s, 'b2': jnp.zeros((H,), dtype=jnp.float32), 'W3': jax.random.normal(ks[6], (H, D), dtype=jnp.float32) * s, 'b3': jnp.zeros((D,), dtype=jnp.float32)}
    _L0_gnn_all = _L0_gnn_setup()
    _L0_gnn_in = {k: v for k, v in _L0_gnn_all.items() if k in ('Wg', 'Ws', 'bg', 'W1', 'b1', 'W2', 'b2', 'W3', 'b3')}
    del _L0_gnn_all
    return {'x': x, 'src': src, 'dst': dst, 'L0_gnn_Wg': _L0_gnn_in['Wg'], 'L0_gnn_Ws': _L0_gnn_in['Ws'], 'L0_gnn_bg': _L0_gnn_in['bg'], 'L0_gnn_W1': _L0_gnn_in['W1'], 'L0_gnn_b1': _L0_gnn_in['b1'], 'L0_gnn_W2': _L0_gnn_in['W2'], 'L0_gnn_b2': _L0_gnn_in['b2'], 'L0_gnn_W3': _L0_gnn_in['W3'], 'L0_gnn_b3': _L0_gnn_in['b3']}

def reference(x, src, dst, L0_gnn_Wg, L0_gnn_Ws, L0_gnn_bg, L0_gnn_W1, L0_gnn_b1, L0_gnn_W2, L0_gnn_b2, L0_gnn_W3, L0_gnn_b3):
    import jax
    import jax.numpy as jnp

    def _L0_gnn_ref(z, edge_index, Wg, Ws, bg, W1, b1, W2, b2, W3, b3):
        import jax, jax.numpy as jnp
        import numpy as np
        N, E, D, H = (12500, 75000, 128, 512)
        src, dst = (edge_index[0], edge_index[1])
        n = z.shape[0]
        msgs = z[src]
        agg = jax.ops.segment_sum(msgs, dst, num_segments=n)
        deg = jax.ops.segment_sum(jnp.ones((src.shape[0],), z.dtype), dst, num_segments=n)
        agg = agg / jnp.maximum(deg, 1.0)[:, None]
        h = jax.nn.relu(agg @ Wg + z @ Ws + bg)
        h = jnp.tanh(h @ W1 + b1)
        h = jnp.tanh(h @ W2 + b2)
        return h @ W3 + b3
    edge_index = jnp.stack([src, dst])
    h = jnp.maximum(_layernorm(x, axis=-1), 0.0)
    x = x + _L0_gnn_ref(h, edge_index, L0_gnn_Wg, L0_gnn_Ws, L0_gnn_bg, L0_gnn_W1, L0_gnn_b1, L0_gnn_W2, L0_gnn_b2, L0_gnn_W3, L0_gnn_b3)
    return x

_drawn_inputs = setup_inputs


def setup_inputs(seed=0):
    import zlib

    import numpy as np

    out = dict(_drawn_inputs(seed))
    spreads = {'L0_gnn_bg': (0.0, 0.1),
     'L0_gnn_b1': (0.0, 0.1),
     'L0_gnn_b2': (0.0, 0.1),
     'L0_gnn_b3': (0.0, 0.1)}
    factors = {}
    for name, (base, spread) in spreads.items():
        noise = np.random.default_rng([zlib.crc32(name.encode()), seed]).standard_normal(out[name].shape)
        drawn = base * np.exp(spread * noise) if base else spread * noise
        out[name] = jnp.asarray(drawn.astype(out[name].dtype))
    for name, factor in factors.items():
        out[name] = (out[name] * factor).astype(out[name].dtype)
    return out
```

```python
from contextlib import ExitStack

import numpy as np

import concourse.bass as bass
from concourse import mybir

ALU = mybir.AluOpType
ACT = mybir.ActivationFunctionType
AX = mybir.AxisListType
F32 = mybir.dt.float32
F16 = mybir.dt.float16
I32 = mybir.dt.int32

P = 128
ROWS = 8
GT = 8
GPI = 4
BLK = 256
LAG = 2
SCALE = 1024.0
EPS = 1e-5


def at(eng, sem, value):
    if not isinstance(value, int) or value > 0:
        eng.wait_ge(sem, value)


def gnn_program(nc, x, src, dst, Wg, Ws, bg, W1, b1, W2, b2, W3, b3, out):
    N, D = x.shape
    E = src.shape[0]
    H = W1.shape[1]
    HC = H // P
    NT = BLK // P
    TILES = -(-E // P)
    GROUPS = -(-TILES // GT)
    ITERS = -(-GROUPS // GPI)
    BLOCKS = -(-N // BLK)
    NPAD = N + P
    WINDOWS = N // P + 1
    CHUNK = P * ROWS
    CHUNKS = N // CHUNK
    REST = N - CHUNKS * CHUNK
    IC = -(-TILES // P)
    FULLQ = (E // P) - (IC - 1) * P
    ODD = E % P
    assert D == P and GROUPS == GPI * ITERS and BLOCKS == ITERS and CHUNKS % 2 == 0 and REST % 2 == 0
    assert ITERS > 4 and ODD and (ITERS + 1) * BLK > NPAD - P

    def tiles_in(g):
        return min(GT, TILES - g * GT) if isinstance(g, int) else GT

    with ExitStack() as ctx:
        def sb(name, shape, dt):
            return ctx.enter_context(nc.sbuf_tensor(name, shape, dt))

        def sem(name):
            return ctx.enter_context(nc.semaphore(name))

        table = nc.dram_tensor("h_table", (N, 2 * D), F16, kind="Internal").ap()

        wg = sb("wg", [P, D], F32)
        ws = sb("ws", [P, D], F32)
        w1 = sb("w1", [P, H], F32)
        w2 = sb("w2", [P, HC, H], F32)
        w3 = sb("w3", [P, HC, D], F32)
        bgc = sb("bgc", [P, 1], F32)
        b1c = sb("b1c", [P, HC], F32)
        b2c = sb("b2c", [P, HC], F32)
        b3r = sb("b3r", [1, D], F32)
        ident = sb("ident", [P, P], F32)
        ident16 = sb("ident16", [P, P], F16)
        iota = sb("iota", [P, P], F32)
        ones32 = sb("ones32", [1, P], F32)
        ones16 = sb("ones16", [P, P], F16)
        dense = sb("dense", [P, (2 * HC + 5) * BLK + NT * D], F32)
        msgs = sb("msgs", [P, GPI, GT, 2 * D], F16)
        stage = dense[:, 0:2 * IC * P].bitcast(I32).rearrange("p (k c e) -> p k c e", k=2, c=IC)
        stagef = msgs[:].rearrange("p r j d -> p (r j d)").bitcast(F32)[:, 0:2 * IC * P].rearrange(
            "p (k c e) -> p k c e", k=2, c=IC)
        idx_all = sb("idx_all", [P, GROUPS * GT], I32)
        dst_all = sb("dst_all", [P, IC * P], F32)
        rel_all = sb("rel_all", [P, GROUPS * GT], F32)
        base_row = sb("base_row", [1, GROUPS], I32)
        limit = sb("limit", [P, GROUPS], F32)
        late = sb("late", [P, GROUPS], F32)
        excess = sb("excess", [P, 4], F32)
        worst = sb("worst", [P, 1], F32)
        verdict = sb("verdict", [1, 1], F32)
        general = sb("general", [1, 1], I32)
        far = sb("far", [P, 1], F32)
        idx_slot = sb("idx_slot", [P, GPI, GT], I32)
        xin = sb("xin", [P, 2, ROWS, D], F32)
        hval = sb("hval", [P, 2, ROWS, D], F32)
        pair = sb("pair", [P, 2, ROWS, 2 * D], F16)
        stats = sb("stats", [P, 2, ROWS, 6], F32)
        moments = sb("moments", [P, 2, ROWS, 2], F32)
        sdev = sb("sdev", [P, 2, ROWS], F32)
        eps = sb("eps", [P, 1], F32)
        scale = sb("scale", [P, 2, ROWS], F32)
        shift = sb("shift", [P, 2, ROWS], F32)
        onehot = sb("onehot", [P, 2, GT, P], F16)
        sums = sb("sums", [P, 2, NPAD], F32)
        xblk = sb("xblk", [P, NT, D], F32)
        tblk = sb("tblk", [P, NT, 2 * D], F16)
        h2T = dense[:, 0:HC * BLK].rearrange("p (c n) -> p c n", c=HC)
        h3T = dense[:, HC * BLK:2 * HC * BLK].rearrange("p (c n) -> p c n", c=HC)
        hownT, count, share, meanT, h1T = (dense[:, (2 * HC + k) * BLK:(2 * HC + k + 1) * BLK] for k in range(5))
        oblk = dense[:, (2 * HC + 5) * BLK:].rearrange("p (t d) -> p t d", t=NT)

        banks = ctx.enter_context(nc.psum_tensor("banks", [P, 8, 512], F32))
        seg_ps = [banks[:, b, 0:2 * P].rearrange("p (k w) -> p k w", k=2) for b in range(2)]
        own_ps = banks[:, 2, 0:BLK]
        out_ps = banks[:, 2, BLK:2 * BLK].rearrange("p (t d) -> p t d", t=NT)
        l1_ps = banks[:, 3, 0:BLK]
        l2_ps = [banks[:, 4 + c // 2, (c % 2) * BLK:(c % 2 + 1) * BLK] for c in range(HC)]
        l3_ps = [banks[:, 6 + c // 2, (c % 2) * BLK:(c % 2 + 1) * BLK] for c in range(HC)]
        turn_ps = [banks[:, b, :] for b in (4, 5, 6, 7, 0, 1, 2, 3)]
        excess_ps = banks[0:1, 5, 0:P]
        base_ps = banks[:, 4, 0:GROUPS]

        weights_in = sem("weights_in")
        stage_padded = sem("stage_padded")
        src_in = sem("src_in")
        dst_in = sem("dst_in")
        stage_cast = sem("stage_cast")
        ident_zero = sem("ident_zero")
        ident_ready = sem("ident_ready")
        consts_ready = sem("consts_ready")
        eps_ready = sem("eps_ready")
        sums_clear = sem("sums_clear")
        turned = sem("turned")
        idx_turned = sem("idx_turned")
        dst_turned = sem("dst_turned")
        base_spread = sem("base_spread")
        base_ready = sem("base_ready")
        rel_ready = sem("rel_ready")
        excess_part = sem("excess_part")
        worst_ready = sem("worst_ready")
        excess_turned = sem("excess_turned")
        verdict_ready = sem("verdict_ready")
        general_ready = sem("general_ready")
        sums_cleared = sem("sums_cleared")
        gen_idx_ready = sem("gen_idx_ready")
        gen_issuing = sem("gen_issuing")
        gen_gathered = sem("gen_gathered")
        gen_far = sem("gen_far")
        gen_onehot = sem("gen_onehot")
        gen_seg = sem("gen_seg")
        gen_added = sem("gen_added")
        gen_through = sem("gen_through")
        x_in = [sem(f"x_in{s}") for s in range(2)]
        stats_done = sem("stats_done")
        moments_done = sem("moments_done")
        sdev_ready = sem("sdev_ready")
        scale_done = sem("scale_done")
        shift_ready = sem("shift_ready")
        scaled = sem("scaled")
        high_ready = sem("high_ready")
        pair_ready = sem("pair_ready")
        table_in = [sem(f"table_in{s}") for s in range(2)]
        idx_ready = sem("idx_ready")
        issuing = sem("issuing")
        gathered = [sem(f"gathered{r}") for r in range(GPI)]
        onehot_ready = sem("onehot_ready")
        seg_done = sem("seg_done")
        added = sem("added")
        xblk_in = sem("xblk_in")
        tblk_in = sem("tblk_in")
        aggr_gate = sem("aggr_gate")
        own_turned = sem("own_turned")
        hownT_ready = sem("hownT_ready")
        count_ready = sem("count_ready")
        share_ready = sem("share_ready")
        mean_ready = sem("mean_ready")
        l1_done = sem("l1_done")
        h1_ready = sem("h1_ready")
        l2_done = sem("l2_done")
        h2_ready = sem("h2_ready")
        l3_done = sem("l3_done")
        h3_ready = sem("h3_ready")
        l4_done = sem("l4_done")
        oblk_ready = sem("oblk_ready")
        out_in = sem("out_in")

        x_chunk = x[0:CHUNKS * CHUNK, :].rearrange("(c p r) d -> c p r d", p=P, r=ROWS)
        t_chunk = table[0:CHUNKS * CHUNK, :].rearrange("(c p r) d -> c p r d", p=P, r=ROWS)
        RP, RR = REST // 2, 2
        x_rest = x[CHUNKS * CHUNK:N, :].rearrange("(p r) d -> p r d", r=RR)
        t_rest = table[CHUNKS * CHUNK:N, :].rearrange("(p r) d -> p r d", r=RR)

        def chunk_shape(c):
            return (RP, RR) if isinstance(c, int) and c == CHUNKS else (P, ROWS)

        def over_chunks(eng, step):
            for c in range(2):
                step(c, 0, c)
            with eng.Fori(1, CHUNKS // 2) as pr:
                for s in range(2):
                    step(2 * pr + s, pr, s)
            step(CHUNKS, CHUNKS // 2, 0)

        def over_iterations(eng, step):
            for it in range(LAG + 1):
                step(it, it - LAG if it >= LAG else None)
            with eng.Fori(LAG + 1, ITERS - 1) as it:
                step(it, it - LAG)
            step(ITERS - 1, ITERS - 1 - LAG)

        def over_blocks(eng, step):
            step(0, 0)
            with eng.Fori(1, BLOCKS - 1) as m:
                step(m, m)
            step(BLOCKS - 1, BLOCKS - 1)

        def again_over_blocks(eng, step):
            with eng.Fori(0, BLOCKS - 1) as m:
                step(m, m + BLOCKS)
            step(BLOCKS - 1, 2 * BLOCKS - 1)

        def is_general(eng):
            eng.wait_ge(general_ready, 1)
            return eng.value_load(general[0:1, 0:1], min_val=0, max_val=1) > 0

        def block_rows(m):
            if isinstance(m, int) and m == BLOCKS - 1:
                left = N - m * BLK
                return [(t, min(P, left - t * P)) for t in range(NT) if left > t * P]
            return None

        block = ctx.enter_context(nc.Block())

        @block.sync
        def _(sp):
            for k, (a, s) in enumerate(((src, src_in), (dst, dst_in))):
                sp.dma_start(stage[:, k, 0:IC - 1, :],
                             a[0:(IC - 1) * P * P].rearrange("(c q e) -> q c e", q=P, e=P)).then_inc(s, 16)
                sp.wait_ge(stage_padded, k + 1)
                sp.dma_start(stage[0:FULLQ, k, IC - 1, :],
                             a[(IC - 1) * P * P:E - ODD].rearrange("(q e) -> q e", e=P)).then_inc(s, 16)
                sp.dma_start(stage[FULLQ:FULLQ + 1, k, IC - 1, 0:ODD],
                             a[E - ODD:E].rearrange("(q e) -> q e", q=1)).then_inc(s, 16)
                if k == 0:
                    for c in range(2):
                        sp.dma_start(xin[:, c], x_chunk[c]).then_inc(x_in[c], 16)

            def table_step(c, pr, s):
                more = not isinstance(c, int) or c + 2 <= CHUNKS
                if more:
                    sp.wait_ge(scaled, c + 1)
                    if isinstance(c, int) and c + 2 == CHUNKS:
                        sp.dma_start(xin[0:RP, s, 0:RR], x_rest).then_inc(x_in[s], 16)
                    else:
                        sp.dma_start(xin[:, s], x_chunk[c + 2]).then_inc(x_in[s], 16)
                sp.wait_ge(pair_ready, c + 1)
                p, r = chunk_shape(c)
                to = t_rest if (p, r) != (P, ROWS) else t_chunk[c]
                sp.dma_start(to, pair[0:p, s, 0:r]).then_inc(table_in[s], 16)

            for c in range(2):
                table_step(c, 0, c)
            with sp.Fori(1, CHUNKS // 2 - 1) as pr:
                for s in range(2):
                    table_step(2 * pr + s, pr, s)
            for c in range(CHUNKS - 2, CHUNKS + 1):
                table_step(c, c // 2, c % 2)

            def dense_io(m, k):
                parts = block_rows(m) or [(0, BLK)]
                inc = 16 * NT // len(parts)

                def rows(dram, t, n):
                    if n == BLK:
                        return dram[bass.ds(m * BLK, BLK), :].rearrange("(t p) d -> p t d", t=NT)
                    return dram[m * BLK + t * P:m * BLK + t * P + n, :]

                def held(buf, t, n):
                    return buf[:] if n == BLK else buf[0:n, t]

                at(sp, oblk_ready, k)
                for t, n in parts:
                    sp.dma_start(held(tblk, t, n), rows(table, t, n)).then_inc(tblk_in, inc)
                for t, n in parts:
                    sp.dma_start(held(xblk, t, n), rows(x, t, n)).then_inc(xblk_in, inc)
                sp.wait_ge(oblk_ready, k + 1)
                for t, n in parts:
                    sp.dma_start(rows(out, t, n), held(oblk, t, n)).then_inc(out_in, inc)

            for s in range(2):
                sp.wait_ge(table_in[s], 16 * ((CHUNKS + 2 - s) // 2))
            over_blocks(sp, dense_io)
            sp.wait_ge(out_in, 16 * NT * BLOCKS)
            with sp.If(is_general(sp)):
                again_over_blocks(sp, dense_io)
                sp.wait_ge(out_in, 2 * 16 * NT * BLOCKS)

        @block.gpsimd
        def _(pool):
            nc.gpsimd.memset(stage[:, 0, IC - 1, :], 0).then_inc(stage_padded, 1)
            nc.gpsimd.memset(stage[:, 1, IC - 1, :], N).then_inc(stage_padded, 1)
            nc.gpsimd.memset(ident[:], 0.0).then_inc(ident_zero, 1)
            pool.wait_ge(ident_zero, 1)
            nc.gpsimd.affine_select(out=ident[:], in_=ident[:], compare_op=ALU.not_equal, fill=1.0, base=0,
                                    pattern=[[-1, P]], channel_multiplier=1).then_inc(ident_ready, 1)
            nc.gpsimd.memset(eps[:], EPS / SCALE ** 2).then_inc(eps_ready, 1)
            pool.wait_ge(ident_ready, 1)
            for k, s in enumerate((src_in, dst_in)):
                pool.wait_ge(s, 48)
                nc.gpsimd.tensor_copy(stagef[:, k], stage[:, k]).then_inc(stage_cast, 1)
            nc.gpsimd.iota(iota[:], pattern=[[1, P]], base=0, channel_multiplier=0,
                           allow_small_or_imprecise_dtypes=True).then_inc(consts_ready, 1)
            nc.gpsimd.tensor_copy(ident16[:], ident[:]).then_inc(consts_ready, 1)
            nc.gpsimd.memset(ones32[:], 1.0).then_inc(consts_ready, 1)
            nc.gpsimd.memset(ones16[:], 1.0).then_inc(consts_ready, 1)
            nc.gpsimd.iota(limit[:], pattern=[[BLK, ITERS], [0, GPI]], base=BLK * (1 - LAG), channel_multiplier=0,
                           allow_small_or_imprecise_dtypes=True).then_inc(consts_ready, 1)
            nc.gpsimd.memset(sums[:], 0.0).then_inc(sums_clear, 1)
            for s in range(2):
                pool.wait_ge(table_in[s], 16 * ((CHUNKS + 2 - s) // 2))
            pool.wait_ge(turned, 2 * -(-IC // 4))

            def gather_step(it, m):
                for r in range(GPI):
                    g = GPI * it + r
                    pool.wait_ge(idx_ready, g + 1)
                    pool.sem_inc(issuing)
                    for j in range(tiles_in(g)):
                        nc.gpsimd.indirect_dma_start(
                            out=msgs[:, r, j, :], out_offset=None, in_=table,
                            in_offset=bass.IndirectOffsetOnAxis(ap=idx_slot[:, r, j:j + 1], axis=0),
                        ).then_inc(gathered[r], 16)

            over_iterations(pool, gather_step)
            with pool.If(is_general(pool)):
                with pool.Fori(0, TILES) as t:
                    pool.wait_ge(gen_idx_ready, t + 1)
                    pool.sem_inc(gen_issuing)
                    nc.gpsimd.indirect_dma_start(
                        out=msgs[:, 0, 0, :], out_offset=None, in_=table,
                        in_offset=bass.IndirectOffsetOnAxis(ap=idx_slot[:, 0, 0:1], axis=0),
                    ).then_inc(gen_gathered, 16)

        @block.tensor
        def _(pe):
            pe.wait_ge(ident_ready, 1)
            b = 0
            for k in range(2):
                pe.wait_ge(stage_cast, k + 1)
                for c0 in range(0, IC, 4):
                    for c in range(c0, min(c0 + 4, IC)):
                        mm = nc.tensor.transpose(turn_ps[b][:, (c - c0) * P:(c - c0 + 1) * P],
                                                 stagef[:, k, c, :], ident[:])
                    mm.then_inc(turned, 1)
                    b += 1
            pe.wait_ge(idx_turned, 1)
            pe.wait_ge(dst_turned, -(-IC // 4))
            pe.wait_ge(consts_ready, 5)
            nc.tensor.matmul(base_ps, ones32[:], dst_all[0:1, 0:GROUPS * GT:GT],
                             start=True, stop=True).then_inc(base_spread, 1)
            pe.wait_ge(weights_in, 16 * 9)
            pe.wait_ge(worst_ready, 1)
            nc.tensor.matmul(excess_ps, worst[:], ident[:], start=True, stop=True).then_inc(excess_turned, 1)
            pe.wait_ge(general_ready, 1)

            def segment(it, r):
                g = GPI * it + r
                b = r % 2
                n = tiles_in(g)
                at(pe, added, g - 1)
                pe.wait_ge(onehot_ready, g + 1)
                for j in range(n):
                    if j == 0:
                        pe.wait_ge(gathered[r], 16 * GT * it + 16 * n)
                    for half in range(2):
                        nc.tensor.matmul(seg_ps[b][:, 0], msgs[:, r, j, half * D:(half + 1) * D],
                                         onehot[:, b, j, :], start=(j == 0 and half == 0),
                                         stop=(j == n - 1 and half == 1))
                for j in range(n):
                    mm = nc.tensor.matmul(seg_ps[b][:, 1], ones16[:], onehot[:, b, j, :],
                                          start=(j == 0), stop=(j == n - 1))
                mm.then_inc(seg_done, 1)

            def turn_own(k):
                pe.wait_ge(tblk_in, 16 * NT * (k + 1))
                at(pe, hownT_ready, k)
                for t in range(NT):
                    for half in range(2):
                        mm = nc.tensor.matmul(own_ps[:, t * P:(t + 1) * P], tblk[:, t, half * D:(half + 1) * D],
                                              ident16[:], start=(half == 0), stop=(half == 1))
                mm.then_inc(own_turned, 1)

            def layer1(k):
                pe.wait_ge(hownT_ready, k + 1)
                nc.tensor.matmul(l1_ps, ws[:], hownT[:], start=True, stop=False)
                pe.wait_ge(mean_ready, k + 1)
                nc.tensor.matmul(l1_ps, wg[:], meanT[:], start=False, stop=True).then_inc(l1_done, 1)

            def layer2(k):
                pe.wait_ge(h1_ready, k + 1)
                for c in range(HC):
                    mm = nc.tensor.matmul(l2_ps[c], w1[:, c * P:(c + 1) * P], h1T[:], start=True, stop=True)
                    if c % 2:
                        mm.then_inc(l2_done, 1)

            def layer3(k):
                pe.wait_ge(h2_ready, HC * (k + 1))
                for c in range(HC):
                    for q in range(HC):
                        mm = nc.tensor.matmul(l3_ps[c], w2[:, q, c * P:(c + 1) * P], h2T[:, q],
                                              start=(q == 0), stop=(q == HC - 1))
                    if c % 2:
                        mm.then_inc(l3_done, 1)

            def layer4(k):
                at(pe, oblk_ready, k)
                for t in range(NT):
                    nc.tensor.matmul(out_ps[:, t], ones32[:], b3r[:], start=True, stop=False)
                    if t == 0:
                        pe.wait_ge(h3_ready, HC * (k + 1))
                    for q in range(HC):
                        mm = nc.tensor.matmul(out_ps[:, t], h3T[:, q, t * P:(t + 1) * P], w3[:, q],
                                              start=False, stop=(q == HC - 1))
                mm.then_inc(l4_done, 1)

            def dense_block(m, k):
                turn_own(k)
                layer1(k)
                layer2(k)
                layer3(k)
                layer4(k)

            def step(it, m):
                segment(it, 0)
                if m is not None:
                    turn_own(m)
                segment(it, 1)
                if m is not None:
                    layer1(m)
                segment(it, 2)
                if m is not None:
                    layer2(m)
                segment(it, 3)
                if m is not None:
                    layer3(m)
                    layer4(m)

            over_iterations(pe, step)
            for m in range(ITERS - LAG, BLOCKS):
                dense_block(m, m)

            with pe.If(is_general(pe)):
                pe.wait_ge(sums_cleared, 1)
                with pe.Fori(0, TILES) as t:
                    with pe.Fori(0, WINDOWS) as w:
                        pe.wait_ge(gen_gathered, 16 * (t + 1))
                        pe.wait_ge(gen_onehot, t * WINDOWS + w + 1)
                        for half in range(2):
                            nc.tensor.matmul(seg_ps[0][:, 0], msgs[:, 0, 0, half * D:(half + 1) * D],
                                             onehot[:, 0, 0, :], start=(half == 0), stop=(half == 1))
                        nc.tensor.matmul(seg_ps[0][:, 1], ones16[:], onehot[:, 0, 0, :],
                                         start=True, stop=True).then_inc(gen_seg, 1)
                again_over_blocks(pe, dense_block)

        @block.scalar
        def _(act):
            for to, frm in ((wg[:], Wg), (ws[:], Ws), (w1[:], W1),
                            (w2[:], W2.rearrange("(k p) n -> p k n", p=P)),
                            (w3[:], W3.rearrange("(k p) n -> p k n", p=P)),
                            (bgc[:], bg.rearrange("(p o) -> p o", o=1)),
                            (b1c[:], b1.rearrange("(c p) -> p c", p=P)),
                            (b2c[:], b2.rearrange("(c p) -> p c", p=P)),
                            (b3r[:], b3.rearrange("(o d) -> o d", o=1))):
                act.dma_start(to, frm, allow_slow_non_contiguous=frm is not W1).then_inc(weights_in, 16)

            def table_sdev(c, s):
                p, rows = chunk_shape(c)
                act.wait_ge(moments_done, c + 1)
                nc.scalar.activation(sdev[0:p, s, 0:rows], moments[0:p, s, 0:rows, 1], ACT.Sqrt,
                                     bias=eps[0:p, 0:1], scale=1 / SCALE ** 2).then_inc(sdev_ready, 1)

            def table_scale(c, pr, s):
                p, rows = chunk_shape(c)
                if not isinstance(c, int) or c >= 2:
                    act.wait_ge(pair_ready, c - 1)
                act.wait_ge(shift_ready, c + 1)
                for r in range(rows):
                    ins = nc.scalar.activation(hval[0:p, s, r], xin[0:p, s, r], ACT.Relu,
                                               bias=shift[0:p, s, r:r + 1], scale=scale[0:p, s, r:r + 1])
                ins.then_inc(scaled, 1)
                act.wait_ge(scaled, c + 1)
                at(act, table_in[s], 16 * pr)
                nc.scalar.copy(pair[0:p, s, 0:rows, 0:D], hval[0:p, s, 0:rows]).then_inc(high_ready, 1)

            act.wait_ge(eps_ready, 1)
            table_sdev(0, 0)
            table_sdev(1, 1)
            table_scale(0, 0, 0)
            table_sdev(2, 0)
            table_scale(1, 0, 1)
            table_sdev(3, 1)
            table_scale(2, 1, 0)
            with act.Fori(2, CHUNKS // 2) as pr:
                table_sdev(2 * pr, 0)
                table_scale(2 * pr - 1, pr - 1, 1)
                table_sdev(2 * pr + 1, 1)
                table_scale(2 * pr, pr, 0)
            table_sdev(CHUNKS, 0)
            table_scale(CHUNKS - 1, CHUNKS // 2 - 1, 1)
            table_scale(CHUNKS, CHUNKS // 2, 0)

            nb = -(-IC // 4)
            for q in range(nb):
                n = min(4, IC - 4 * q)
                act.wait_ge(turned, nb + q + 1)
                nc.scalar.copy(dst_all[:, 4 * q * P:(4 * q + n) * P], turn_ps[nb + q][:, 0:n * P]
                               ).then_inc(dst_turned, 1)

            act.wait_ge(weights_in, 16 * 9)

            def dense_block(m, k):
                act.wait_ge(own_turned, k + 1)
                nc.scalar.mul(hownT[:], own_ps, 1 / SCALE).then_inc(hownT_ready, 1)
                act.wait_ge(l1_done, k + 1)
                nc.scalar.activation(h1T[:], l1_ps, ACT.Relu, bias=bgc[:, 0:1]).then_inc(h1_ready, 1)
                for c in range(HC):
                    if c % 2 == 0:
                        act.wait_ge(l2_done, HC // 2 * k + c // 2 + 1)
                    nc.scalar.activation(h2T[:, c], l2_ps[c], ACT.Tanh, bias=b1c[:, c:c + 1]
                                         ).then_inc(h2_ready, 1)
                for c in range(HC):
                    if c % 2 == 0:
                        act.wait_ge(l3_done, HC // 2 * k + c // 2 + 1)
                    nc.scalar.activation(h3T[:, c], l3_ps[c], ACT.Tanh, bias=b2c[:, c:c + 1]
                                         ).then_inc(h3_ready, 1)

            over_blocks(act, dense_block)
            with act.If(is_general(act)):
                again_over_blocks(act, dense_block)

        @block.vector
        def _(dve):
            nb = -(-IC // 4)
            for q in range(nb):
                lo = 4 * q * P
                hi = min(lo + 4 * P, GROUPS * GT)
                dve.wait_ge(turned, q + 1)
                nc.vector.tensor_copy(idx_all[:, lo:hi], turn_ps[q][:, 0:hi - lo]).then_inc(idx_turned, 1)
            dve.wait_ge(idx_turned, nb)
            for g in range(GPI):
                nc.vector.tensor_copy(idx_slot[:, g], idx_all[:, g * GT:(g + 1) * GT]).then_inc(idx_ready, 1)

            def gate(sem_, value):
                if isinstance(value, int):
                    dve.wait_ge(sem_, value)
                else:
                    dve.wait_ge(sem_, value)
                    dve.sem_inc(aggr_gate)

            def table_stats(c, pr, s):
                p, rows = chunk_shape(c)
                dve.wait_ge(x_in[s], 16 * (pr + 1))
                for r in range(rows):
                    ins = nc.vector.bn_stats(stats[0:p, s, r], xin[0:p, s, r])
                ins.then_inc(stats_done, 1)
                gate(stats_done, c + 1)
                for r in range(rows):
                    ins = nc.vector.bn_aggr(moments[0:p, s, r], stats[0:p, s, r])
                ins.then_inc(moments_done, 1)

            def table_shift(c, s):
                p, rows = chunk_shape(c)
                dve.wait_ge(sdev_ready, c + 1)
                nc.vector.reciprocal(scale[0:p, s, 0:rows], sdev[0:p, s, 0:rows]).then_inc(scale_done, 1)
                dve.wait_ge(scale_done, c + 1)
                nc.vector.scalar_tensor_tensor(out=shift[0:p, s, 0:rows], in0=moments[0:p, s, 0:rows, 0],
                                               scalar=-1.0, in1=scale[0:p, s, 0:rows],
                                               op0=ALU.mult, op1=ALU.mult).then_inc(shift_ready, 1)

            def table_low(c, s):
                p, rows = chunk_shape(c)
                dve.wait_ge(high_ready, c + 1)
                nc.vector.tensor_tensor(pair[0:p, s, 0:rows, D:2 * D], hval[0:p, s, 0:rows],
                                        pair[0:p, s, 0:rows, 0:D], ALU.subtract).then_inc(pair_ready, 1)

            table_stats(0, 0, 0)
            table_stats(1, 0, 1)
            table_shift(0, 0)
            with dve.Fori(1, CHUNKS // 2) as pr:
                table_stats(2 * pr, pr, 0)
                table_shift(2 * pr - 1, 1)
                table_low(2 * pr - 2, 0)
                table_stats(2 * pr + 1, pr, 1)
                table_shift(2 * pr, 0)
                table_low(2 * pr - 1, 1)
            table_stats(CHUNKS, CHUNKS // 2, 0)
            table_shift(CHUNKS - 1, 1)
            table_low(CHUNKS - 2, 0)
            table_shift(CHUNKS, 0)
            table_low(CHUNKS - 1, 1)
            table_low(CHUNKS, 0)

            dve.wait_ge(dst_turned, nb)
            nc.vector.tensor_copy(base_row[:], dst_all[0:1, 0:GROUPS * GT:GT]).then_inc(base_ready, 1)
            dve.wait_ge(base_spread, 1)
            nc.vector.tensor_tensor(rel_all[:].rearrange("p (g j) -> p g j", j=GT),
                                    dst_all[:, 0:GROUPS * GT].rearrange("p (g j) -> p g j", j=GT),
                                    base_ps.unsqueeze(2).to_broadcast([P, GROUPS, GT]),
                                    ALU.subtract).then_inc(rel_ready, 1)
            dve.wait_ge(base_ready, 1)
            dve.wait_ge(consts_ready, 5)
            dve.wait_ge(rel_ready, 1)
            nc.vector.tensor_reduce(excess[:, 0:1], rel_all[:], AX.X, ALU.max).then_inc(excess_part, 1)
            nc.vector.tensor_reduce(excess[:, 1:2], rel_all[:], AX.X, ALU.min).then_inc(excess_part, 1)
            nc.vector.tensor_tensor(late[:], limit[:], base_ps, ALU.subtract).then_inc(excess_part, 1)
            dve.wait_ge(excess_part, 3)
            nc.vector.tensor_reduce(excess[:, 2:3], late[:], AX.X, ALU.max).then_inc(excess_part, 1)
            nc.vector.tensor_scalar(excess[:, 0:1], excess[:, 0:1], 1.0 - P, None, ALU.add).then_inc(excess_part, 1)
            nc.vector.tensor_scalar(excess[:, 1:2], excess[:, 1:2], -1.0, None, ALU.mult).then_inc(excess_part, 1)
            dve.wait_ge(excess_part, 6)
            nc.vector.tensor_reduce(worst[:], excess[:, 0:3], AX.X, ALU.max).then_inc(worst_ready, 1)
            dve.wait_ge(excess_turned, 1)
            nc.vector.tensor_reduce(verdict[:], excess_ps, AX.X, ALU.max).then_inc(verdict_ready, 1)
            dve.wait_ge(verdict_ready, 1)
            nc.vector.tensor_scalar(general[:], verdict[:], 0.0, None, ALU.is_gt).then_inc(general_ready, 1)

            def make_onehot(g, b):
                nc.vector.tensor_tensor(onehot[:, b], iota[:].unsqueeze(1).to_broadcast([P, GT, P]),
                                        rel_all[:, bass.ds(g * GT, GT)].unsqueeze(2).to_broadcast([P, GT, P]),
                                        ALU.is_equal).then_inc(onehot_ready, 1)

            def add_sums(g, b):
                base = dve.value_load(base_row[0:1, bass.ds(g, 1)], min_val=0, max_val=N - 1)
                at(dve, added, g)
                dve.wait_ge(seg_done, g + 1)
                window = sums[:, :, bass.ds(base, P)]
                nc.vector.tensor_tensor(window, seg_ps[b], window, ALU.add).then_inc(added, 1)

            def fill_idx(g, r):
                nc.vector.tensor_copy(idx_slot[:, r], idx_all[:, bass.ds(g * GT, GT)]).then_inc(idx_ready, 1)

            def mean(m, k):
                nc.vector.tensor_scalar(count[:], sums[:, 1, bass.ds(m * BLK, BLK)], 1.0, SCALE,
                                        ALU.max, ALU.mult).then_inc(count_ready, 1)
                dve.wait_ge(count_ready, k + 1)
                nc.vector.reciprocal(share[:], count[:]).then_inc(share_ready, 1)
                dve.wait_ge(share_ready, k + 1)
                nc.vector.tensor_tensor(meanT[:], sums[:, 0, bass.ds(m * BLK, BLK)], share[:],
                                        ALU.mult).then_inc(mean_ready, 1)

            def residual(k):
                dve.wait_ge(xblk_in, 16 * NT * (k + 1))
                dve.wait_ge(l4_done, k + 1)
                at(dve, out_in, 16 * NT * k)
                nc.vector.tensor_tensor(oblk[:], out_ps, xblk[:], ALU.add).then_inc(oblk_ready, 1)

            def dense_block(m, k):
                mean(m, k)
                residual(k)

            def step(it, m):
                for r in range(GPI):
                    g = GPI * it + r
                    static = isinstance(g, int)
                    if not static or g > 0:
                        add_sums(g - 1, (r - 1) % 2)
                    if static and g == 0:
                        make_onehot(0, 0)
                    if not static or g + 1 < GROUPS:
                        make_onehot(g + 1, (r + 1) % 2)
                    if not static or 0 < g and g + GPI - 1 < GROUPS:
                        fill_idx(g + GPI - 1, (r + GPI - 1) % GPI)
                    if r == 0 and m is not None:
                        dve.wait_ge(added, g)
                        mean(m, m)
                if m is not None:
                    residual(m)

            dve.wait_ge(sums_clear, 1)
            over_iterations(dve, step)
            add_sums(GROUPS - 1, (GROUPS - 1) % 2)
            dve.wait_ge(added, GROUPS)
            for m in range(ITERS - LAG, BLOCKS):
                dense_block(m, m)

            with dve.If(is_general(dve)):
                nc.vector.memset(sums[:], 0.0).then_inc(sums_cleared, 1)
                dve.wait_ge(sums_cleared, 1)
                with dve.Fori(0, TILES) as t:
                    nc.vector.tensor_copy(idx_slot[:, 0, 0:1], idx_all[:, bass.ds(t, 1)]).then_inc(gen_idx_ready, 1)
                    nc.vector.tensor_copy(far[:], dst_all[:, bass.ds(t, 1)]).then_inc(gen_far, 1)
                    with dve.Fori(0, WINDOWS) as w:
                        dve.wait_ge(gen_far, t * (WINDOWS + 1) + w + 1)
                        nc.vector.tensor_scalar(onehot[:, 0, 0, :], iota[:], far[:, 0:1], None, ALU.is_equal
                                                ).then_inc(gen_onehot, 1)
                        dve.wait_ge(gen_onehot, t * WINDOWS + w + 1)
                        nc.vector.tensor_scalar(far[:], far[:], float(P), None, ALU.subtract).then_inc(gen_far, 1)
                        dve.wait_ge(gen_seg, t * WINDOWS + w + 1)
                        window = sums[:, :, bass.ds(w * P, P)]
                        nc.vector.tensor_tensor(window, seg_ps[0], window, ALU.add).then_inc(gen_added, 1)
                        dve.wait_ge(gen_added, t * WINDOWS + w + 1)
                        dve.sem_inc(gen_through)
                again_over_blocks(dve, dense_block)


_INS = ['x', 'src', 'dst', 'L0_gnn_Wg', 'L0_gnn_Ws', 'L0_gnn_bg', 'L0_gnn_W1', 'L0_gnn_b1',
        'L0_gnn_W2', 'L0_gnn_b2', 'L0_gnn_W3', 'L0_gnn_b3']


def kernel(**inputs):
    import concourse.bacc as _bacc
    from concourse.bass_utils import run_bass_kernel_spmd as _run

    nc = _bacc.Bacc("TRN2", target_bir_lowering=False, num_devices=1)
    arrays, args = {}, []
    for name in _INS:
        a = np.ascontiguousarray(inputs[name])
        arrays[f"in_{name}_dram"] = a
        args.append(nc.dram_tensor(f"in_{name}_dram", a.shape, mybir.dt.from_np(a.dtype), kind="ExternalInput").ap())
    args.append(nc.dram_tensor("out_0_dram", tuple(inputs['x'].shape), F32, kind="ExternalOutput").ap())
    gnn_program(nc, *args)
    r = _run(nc, [arrays], core_ids=[0])
    return r.results[0]["out_0_dram"]
```

```python
from contextlib import ExitStack

import numpy as np

import concourse.bass as bass
from concourse import mybir

ALU = mybir.AluOpType
ACT = mybir.ActivationFunctionType
AX = mybir.AxisListType
F32 = mybir.dt.float32
F16 = mybir.dt.float16
I32 = mybir.dt.int32

P = 128
ROWS = 16
GT = 8
GPI = 4
AHEAD = 2
RAWG = 6
BLK = 256
SPAN = 1024
SCALE = 1024.0
EPS = 1e-5


def at(eng, sem, value):
    if not isinstance(value, int) or value > 0:
        eng.wait_ge(sem, value)


def wait_alone(eng, sem, value, passed):
    eng.wait_ge(sem, value)
    eng.sem_inc(passed)


def gnn_program(nc, x, src, dst, Wg, Ws, bg, W1, b1, W2, b2, W3, b3, out):
    N, D = x.shape
    E = src.shape[0]
    H = W1.shape[1]
    HC = H // P
    NT = BLK // P
    TILES = -(-E // P)
    GROUPS = -(-TILES // GT)
    TURNS = -(-(GROUPS + AHEAD) // GPI)
    BLOCKS = -(-N // BLK)
    CHUNK = P * ROWS
    CHUNKS = N // CHUNK
    REST = N - CHUNKS * CHUNK
    RP, RR = REST // 2, 2
    TC = CHUNKS + 1
    IC = -(-TILES // P)
    FULLQ = (E // P) - (IC - 1) * P
    ODD = E % P
    TB = -(-IC // 4)
    RAWT = RAWG * GT
    assert D == P and TURNS == BLOCKS + 1 and REST and REST % 2 == 0 and ODD and TILES > RAWT + GPI * GT
    assert IC * P >= (GROUPS + 1) * GT
    assert RAWG == 2 * GPI - AHEAD and AHEAD % 2 == 0 and REST <= 2 * P and CHUNKS >= 3

    def tiles_in(g):
        return min(GT, TILES - g * GT) if isinstance(g, int) else GT

    def group(u, r):
        g = GPI * u + r - AHEAD
        return None if isinstance(g, int) and not 0 <= g < GROUPS else g

    with ExitStack() as ctx:
        def sb(name, shape, dt):
            return ctx.enter_context(nc.sbuf_tensor(name, shape, dt))

        def sem(name):
            return ctx.enter_context(nc.semaphore(name))

        table = nc.dram_tensor("h_table", (N, 2 * D), F16, kind="Internal").ap()

        wg = sb("wg", [P, D], F32)
        ws = sb("ws", [P, D], F32)
        w1 = sb("w1", [P, H], F32)
        w2 = sb("w2", [P, HC, H], F32)
        w3 = sb("w3", [P, HC, D], F32)
        bgc = sb("bgc", [P, 1], F32)
        b1c = sb("b1c", [P, HC], F32)
        b2c = sb("b2c", [P, HC], F32)
        b3r = sb("b3r", [1, D], F32)
        ident = sb("ident", [P, P], F32)
        ident16 = sb("ident16", [P, P], F16)
        iota = sb("iota", [P, BLK], F32)
        ones32 = sb("ones32", [1, P], F32)
        ones16 = sb("ones16", [P, P], F16)
        eps = sb("eps", [P, 1], F32)
        dense = sb("dense", [P, (2 * HC + 5) * BLK + NT * D], F32)
        msgs = sb("msgs", [P, GPI, GT, 2 * D], F16)
        stage = dense[:, 0:2 * IC * P].bitcast(I32).rearrange("p (k c e) -> p k c e", k=2, c=IC)
        stagef = msgs[:].rearrange("p r j d -> p (r j d)").bitcast(F32)[:, 0:2 * IC * P].rearrange(
            "p (k c e) -> p k c e", k=2, c=IC)
        raw_idx = sb("raw_idx", [P, RAWG, GT], I32)
        raw_dst = sb("raw_dst", [P, RAWG, GT], I32)
        idx_all = sb("idx_all", [P, IC * P], I32)
        dst_all = sb("dst_all", [P, IC * P], F32)
        rel_all = sb("rel_all", [P, GROUPS * GT], F32)
        base_all = sb("base_all", [P, GROUPS], F32)
        origin = sb("origin", [P, GPI * TURNS], F32)
        offset = sb("offset", [P, GROUPS], F32)
        offset_row = sb("offset_row", [1, GROUPS], I32)
        idx_slot = sb("idx_slot", [P, GPI, GT], I32)
        excess = sb("excess", [P, 4], F32)
        worst = sb("worst", [P, 1], F32)
        verdict = sb("verdict", [1, 1], F32)
        general = sb("general", [1, 1], I32)
        xin = sb("xin", [P, CHUNKS * ROWS + RR, D], F32)
        raw = sb("raw", [P, RAWG, GT, D], F32)
        hval = sb("hval", [P, 2, ROWS, D], F32)
        pair = sb("pair", [P, 2, ROWS, 2 * D], F16)
        stats = sb("stats", [P, 2, ROWS, 6], F32)
        moments = sb("moments", [P, 2, ROWS, 2], F32)
        sdev = sb("sdev", [P, 2, ROWS], F32)
        scale = sb("scale", [P, 2, ROWS], F32)
        shift = sb("shift", [P, 2, ROWS], F32)
        onehot = sb("onehot", [P, 2, GT, P], F16)
        sums = sb("sums", [P, 2, SPAN], F32)
        tblk = sb("tblk", [P, NT, 2 * D], F16)
        xblk = sb("xblk", [P, NT, D], F32)
        h2T = dense[:, 0:HC * BLK].rearrange("p (c n) -> p c n", c=HC)
        h3T = dense[:, HC * BLK:2 * HC * BLK].rearrange("p (c n) -> p c n", c=HC)
        hownT, count, share, meanT, h1T = (dense[:, (2 * HC + k) * BLK:(2 * HC + k + 1) * BLK] for k in range(5))
        oblk = dense[:, (2 * HC + 5) * BLK:].rearrange("p (t d) -> p t d", t=NT)

        banks = ctx.enter_context(nc.psum_tensor("banks", [P, 8, 512], F32))
        seg_ps = [banks[:, b, 0:2 * P].rearrange("p (k w) -> p k w", k=2) for b in range(2)]
        own_ps = banks[:, 2, 0:BLK]
        out_ps = banks[:, 2, BLK:2 * BLK].rearrange("p (t d) -> p t d", t=NT)
        l1_ps = banks[:, 3, 0:BLK]
        l2_ps = [banks[:, 4 + c // 2, (c % 2) * BLK:(c % 2 + 1) * BLK] for c in range(HC)]
        l3_ps = [banks[:, 6 + c // 2, (c % 2) * BLK:(c % 2 + 1) * BLK] for c in range(HC)]
        turn_ps = [banks[:, b, :] for b in (4, 5, 6, 7, 0, 1, 2, 3)]
        excess_ps = banks[0:1, 5, 0:P]
        base_ps = banks[:, 4, 0:GROUPS]
        gen_sum_ps = banks[:, 0, 0:BLK]
        gen_count_ps = banks[:, 1, 0:BLK]

        weights_in = sem("weights_in")
        raw_idx_in = sem("raw_idx_in")
        raw_dst_in = sem("raw_dst_in")
        src_in = sem("src_in")
        dst_in = sem("dst_in")
        stage_padded = sem("stage_padded")
        stage_cast = sem("stage_cast")
        ident_zero = sem("ident_zero")
        ident_ready = sem("ident_ready")
        iota_ready = sem("iota_ready")
        consts_ready = sem("consts_ready")
        turned = sem("turned")
        idx_turned = sem("idx_turned")
        dst_turned = sem("dst_turned")
        dst_ready = sem("dst_ready")
        base_spread = sem("base_spread")
        base_ready = sem("base_ready")
        rel_ready = sem("rel_ready")
        offset_ready = sem("offset_ready")
        excess_part = sem("excess_part")
        worst_ready = sem("worst_ready")
        excess_turned = sem("excess_turned")
        verdict_ready = sem("verdict_ready")
        general_ready = sem("general_ready")
        x_in = [sem(f"x_in{s}") for s in range(TC)]
        raw_in = [sem(f"raw_in{s}") for s in range(RAWG)]
        stats_done = sem("stats_done")
        moments_done = sem("moments_done")
        sdev_ready = sem("sdev_ready")
        scale_done = sem("scale_done")
        shift_ready = sem("shift_ready")
        scaled = sem("scaled")
        high_ready = sem("high_ready")
        pair_ready = sem("pair_ready")
        table_in = [sem(f"table_in{s}") for s in range(2)]
        sums_clear = sem("sums_clear")
        idx_ready = sem("idx_ready")
        issuing = sem("issuing")
        dve_passed = sem("dve_passed")
        gathered = [sem(f"gathered{s}") for s in range(GPI)]
        onehot_ready = sem("onehot_ready")
        seg_done = sem("seg_done")
        added = sem("added")
        moved = sem("moved")
        xblk_in = sem("xblk_in")
        tblk_in = sem("tblk_in")
        own_turned = sem("own_turned")
        hownT_ready = sem("hownT_ready")
        count_ready = sem("count_ready")
        share_ready = sem("share_ready")
        mean_ready = sem("mean_ready")
        l1_done = sem("l1_done")
        h1_ready = sem("h1_ready")
        l2_done = sem("l2_done")
        h2_ready = sem("h2_ready")
        l3_done = sem("l3_done")
        h3_ready = sem("h3_ready")
        l4_done = sem("l4_done")
        oblk_ready = sem("oblk_ready")
        out_in = sem("out_in")
        gen_idx_ready = sem("gen_idx_ready")
        gen_gathered = sem("gen_gathered")
        gen_onehot = sem("gen_onehot")
        gen_seg = sem("gen_seg")
        gen_moved = sem("gen_moved")

        x_chunk = x[0:CHUNKS * CHUNK, :].rearrange("(c p r) d -> c p r d", p=P, r=ROWS)
        t_chunk = table[0:CHUNKS * CHUNK, :].rearrange("(c p r) d -> c p r d", p=P, r=ROWS)
        x_rest = x[CHUNKS * CHUNK:N, :].rearrange("(p r) d -> p r d", r=RR)
        t_rest = table[CHUNKS * CHUNK:N, :].rearrange("(p r) d -> p r d", r=RR)

        def chunk_rows(c):
            if c < CHUNKS:
                return P, ROWS, xin[:, c * ROWS:(c + 1) * ROWS]
            if c == CHUNKS:
                return RP, RR, xin[:, CHUNKS * ROWS:CHUNKS * ROWS + RR]
            return P, GT, raw[:, c - TC]

        def table_whole(eng):
            for s in range(2):
                eng.wait_ge(table_in[s], 16 * ((TC + 1 - s) // 2))

        def over_turns(eng, step):
            for u in range(3):
                step(u, u - 2 if u >= 2 else None)
            with eng.Fori(3, TURNS - 1) as u:
                step(u, u - 2)
            step(TURNS - 1, TURNS - 3)

        def over_blocks(eng, step):
            step(0, 0)
            with eng.Fori(1, BLOCKS - 1) as m:
                step(m, m)
            step(BLOCKS - 1, BLOCKS - 1)

        def again_over_blocks(eng, step):
            with eng.Fori(0, BLOCKS - 1) as m:
                step(m, m + BLOCKS)
            step(BLOCKS - 1, 2 * BLOCKS - 1)

        def over_all_tiles(eng, m, step):
            step(0, m * TILES + 1)
            with eng.Fori(1, TILES - 1) as t:
                step(t, m * TILES + t + 1)
            step(TILES - 1, (m + 1) * TILES)

        def is_general(eng):
            eng.wait_ge(general_ready, 1)
            return eng.value_load(general[0:1, 0:1], min_val=0, max_val=1) > 0

        def block_rows(m):
            if isinstance(m, int) and m == BLOCKS - 1:
                left = N - m * BLK
                return [(t, min(P, left - t * P)) for t in range(NT) if left > t * P]
            return None

        block = ctx.enter_context(nc.Block())

        @block.sync
        def _(sp):
            sp.dma_start(raw_idx[:], src[0:RAWT * P].rearrange("(g p j) -> p g j", p=P, j=GT)
                         ).then_inc(raw_idx_in, 16)
            for c in range(CHUNKS):
                sp.dma_start(xin[:, c * ROWS:(c + 1) * ROWS], x_chunk[c]).then_inc(x_in[c], 16)
            sp.dma_start(xin[0:RP, CHUNKS * ROWS:CHUNKS * ROWS + RR], x_rest).then_inc(x_in[CHUNKS], 16)
            for c in range(TC):
                s = c % 2
                p, rows, _held = chunk_rows(c)
                sp.wait_ge(pair_ready, c + 1)
                sp.dma_start(t_chunk[c] if c < CHUNKS else t_rest, pair[0:p, s, 0:rows]).then_inc(table_in[s], 16)

            def dense_io(m, k):
                parts = block_rows(m) or [(0, BLK)]
                inc = 16 * NT // len(parts)

                def rows(dram, t, n):
                    if n == BLK:
                        return dram[bass.ds(m * BLK, BLK), :].rearrange("(t p) d -> p t d", t=NT)
                    return dram[m * BLK + t * P:m * BLK + t * P + n, :]

                def held(buf, t, n):
                    return buf[:] if n == BLK else buf[0:n, t]

                at(sp, oblk_ready, k)
                for t, n in parts:
                    sp.dma_start(held(tblk, t, n), rows(table, t, n)).then_inc(tblk_in, inc)
                for t, n in parts:
                    sp.dma_start(held(xblk, t, n), rows(x, t, n)).then_inc(xblk_in, inc)
                sp.wait_ge(oblk_ready, k + 1)
                for t, n in parts:
                    sp.dma_start(rows(out, t, n), held(oblk, t, n)).then_inc(out_in, inc)

            table_whole(sp)
            over_blocks(sp, dense_io)
            again = is_general(sp)
            sp.wait_ge(out_in, 16 * NT * BLOCKS)
            with sp.If(again):
                again_over_blocks(sp, dense_io)
                sp.wait_ge(out_in, 2 * 16 * NT * BLOCKS)

        @block.gpsimd
        def _(pool):
            nc.gpsimd.memset(ident[:], 0.0).then_inc(ident_zero, 1)
            pool.wait_ge(ident_zero, 1)
            nc.gpsimd.affine_select(out=ident[:], in_=ident[:], compare_op=ALU.not_equal, fill=1.0, base=0,
                                    pattern=[[-1, P]], channel_multiplier=1).then_inc(ident_ready, 1)
            nc.gpsimd.iota(iota[:], pattern=[[1, BLK]], base=0, channel_multiplier=0,
                           allow_small_or_imprecise_dtypes=True).then_inc(iota_ready, 1)
            pool.wait_ge(ident_ready, 1)
            nc.gpsimd.tensor_copy(ident16[:], ident[:]).then_inc(ident_ready, 1)
            nc.gpsimd.iota(origin[:], pattern=[[BLK, TURNS], [0, GPI]], base=-BLK, channel_multiplier=0,
                           allow_small_or_imprecise_dtypes=True).then_inc(iota_ready, 1)

            pool.wait_ge(raw_idx_in, 16)
            for g in range(RAWG):
                for j in range(GT):
                    nc.gpsimd.indirect_dma_start(
                        out=raw[:, g, j, :], out_offset=None, in_=x,
                        in_offset=bass.IndirectOffsetOnAxis(ap=raw_idx[:, g, j:j + 1], axis=0),
                    ).then_inc(raw_in[g], 16)

            table_whole(pool)
            pool.wait_ge(turned, 2 * TB)

            def gather_step(u, m):
                for r in range(GPI):
                    g = group(u, r)
                    if g is None or isinstance(g, int) and g < RAWG:
                        continue
                    wait_alone(pool, idx_ready, g - RAWG + 1, issuing)
                    for j in range(tiles_in(g)):
                        nc.gpsimd.indirect_dma_start(
                            out=msgs[:, r, j, :], out_offset=None, in_=table,
                            in_offset=bass.IndirectOffsetOnAxis(ap=idx_slot[:, r, j:j + 1], axis=0),
                        ).then_inc(gathered[r], 16)

            over_turns(pool, gather_step)

            with pool.If(is_general(pool)):
                def gather_tile(t, n):
                    wait_alone(pool, gen_idx_ready, n, issuing)
                    nc.gpsimd.indirect_dma_start(
                        out=msgs[:, 0, 0, :], out_offset=None, in_=table,
                        in_offset=bass.IndirectOffsetOnAxis(ap=idx_slot[:, 0, 0:1], axis=0),
                    ).then_inc(gen_gathered, 16)

                with pool.Fori(0, BLOCKS) as m:
                    over_all_tiles(pool, m, gather_tile)

        @block.tensor
        def _(pe):
            pe.wait_ge(ident_ready, 1)
            for b in range(2 * TB):
                k, c0 = b // TB, b % TB * 4
                pe.wait_ge(stage_cast, k + 1)
                for c in range(c0, min(c0 + 4, IC)):
                    mm = nc.tensor.transpose(turn_ps[b][:, (c - c0) * P:(c - c0 + 1) * P],
                                             stagef[:, k, c, :], ident[:])
                mm.then_inc(turned, 1)
            pe.wait_ge(idx_turned, TB)
            pe.wait_ge(dst_ready, 1)
            pe.wait_ge(consts_ready, 1)
            nc.tensor.matmul(base_ps, ones32[:], dst_all[0:1, 0:GROUPS * GT:GT],
                             start=True, stop=True).then_inc(base_spread, 1)

            def segment(u, r):
                g = group(u, r)
                if g is None:
                    return
                b = r % 2
                n = tiles_in(g)
                if isinstance(g, int) and g < RAWG:
                    rows = pair[:, (TC + g) % 2]
                    arrived, count_in = pair_ready, TC + g + 1
                else:
                    rows = msgs[:, r]
                    arrived, count_in = gathered[r], 16 * GT * (u - 2) + 16 * n
                at(pe, added, g - 1)
                pe.wait_ge(onehot_ready, g + 1)
                pe.wait_ge(arrived, count_in)
                for j in range(n):
                    for half in range(2):
                        nc.tensor.matmul(seg_ps[b][:, 0], rows[:, j, half * D:(half + 1) * D],
                                         onehot[:, b, j, :], start=(j == 0 and half == 0),
                                         stop=(j == n - 1 and half == 1))
                for j in range(n):
                    mm = nc.tensor.matmul(seg_ps[b][:, 1], ones16[:], onehot[:, b, j, :],
                                          start=(j == 0), stop=(j == n - 1))
                mm.then_inc(seg_done, 1)

            def turn_own(k):
                pe.wait_ge(tblk_in, 16 * NT * (k + 1))
                at(pe, hownT_ready, k)
                for t in range(NT):
                    for half in range(2):
                        mm = nc.tensor.matmul(own_ps[:, t * P:(t + 1) * P], tblk[:, t, half * D:(half + 1) * D],
                                              ident16[:], start=(half == 0), stop=(half == 1))
                mm.then_inc(own_turned, 1)

            def layer1(k):
                pe.wait_ge(hownT_ready, k + 1)
                nc.tensor.matmul(l1_ps, ws[:], hownT[:], start=True, stop=False)
                pe.wait_ge(mean_ready, k + 1)
                nc.tensor.matmul(l1_ps, wg[:], meanT[:], start=False, stop=True).then_inc(l1_done, 1)

            def layer2(k):
                pe.wait_ge(h1_ready, k + 1)
                for c in range(HC):
                    mm = nc.tensor.matmul(l2_ps[c], w1[:, c * P:(c + 1) * P], h1T[:], start=True, stop=True)
                    if c % 2:
                        mm.then_inc(l2_done, 1)

            def layer3(k):
                pe.wait_ge(h2_ready, HC * (k + 1))
                for c in range(HC):
                    for q in range(HC):
                        mm = nc.tensor.matmul(l3_ps[c], w2[:, q, c * P:(c + 1) * P], h2T[:, q],
                                              start=(q == 0), stop=(q == HC - 1))
                    if c % 2:
                        mm.then_inc(l3_done, 1)

            def layer4(k):
                at(pe, oblk_ready, k)
                for t in range(NT):
                    nc.tensor.matmul(out_ps[:, t], ones32[:], b3r[:], start=True, stop=False)
                    if t == 0:
                        pe.wait_ge(h3_ready, HC * (k + 1))
                    for q in range(HC):
                        mm = nc.tensor.matmul(out_ps[:, t], h3T[:, q, t * P:(t + 1) * P], w3[:, q],
                                              start=False, stop=(q == HC - 1))
                mm.then_inc(l4_done, 1)

            def general_sums(m):
                def sum_tile(t, n):
                    first = isinstance(t, int) and t == 0
                    last = isinstance(t, int) and t == TILES - 1
                    pe.wait_ge(gen_gathered, 16 * n)
                    pe.wait_ge(gen_onehot, n)
                    to_nodes = onehot[:, 0, 0:NT, :].rearrange("p t w -> p (t w)")
                    for half in range(2):
                        nc.tensor.matmul(gen_sum_ps, msgs[:, 0, 0, half * D:(half + 1) * D], to_nodes,
                                         start=(first and half == 0), stop=(last and half == 1))
                    nc.tensor.matmul(gen_count_ps, ones16[:], to_nodes, start=first, stop=last
                                     ).then_inc(gen_seg, 1)

                over_all_tiles(pe, m, sum_tile)

            def dense_block(m, k):
                turn_own(k)
                layer1(k)
                layer2(k)
                layer3(k)
                layer4(k)

            def step(u, m):
                segment(u, 0)
                if m is not None:
                    turn_own(m)
                segment(u, 1)
                if m is not None:
                    layer1(m)
                segment(u, 2)
                if m is not None:
                    layer2(m)
                segment(u, 3)
                if m is not None:
                    layer3(m)
                    layer4(m)
                if isinstance(u, int) and u == 1:
                    pe.wait_ge(weights_in, 16 * 9)
                    pe.wait_ge(worst_ready, 1)
                    nc.tensor.matmul(excess_ps, worst[:], ident[:], start=True, stop=True
                                     ).then_inc(excess_turned, 1)
                    pe.wait_ge(general_ready, 1)

            pe.wait_ge(dst_turned, TB)
            pe.wait_ge(ident_ready, 2)
            over_turns(pe, step)
            dense_block(BLOCKS - 1, BLOCKS - 1)

            with pe.If(is_general(pe)):
                with pe.Fori(0, BLOCKS - 1) as m:
                    general_sums(m)
                    dense_block(m, m + BLOCKS)
                general_sums(BLOCKS - 1)
                dense_block(BLOCKS - 1, 2 * BLOCKS - 1)

        @block.scalar
        def _(act):
            act.dma_start(raw_dst[:], dst[0:RAWT * P].rearrange("(g p j) -> p g j", p=P, j=GT)
                          ).then_inc(raw_dst_in, 16)
            for k, (a, s) in enumerate(((src, src_in), (dst, dst_in))):
                act.dma_start(stage[:, k, 0:IC - 1, :],
                              a[0:(IC - 1) * P * P].rearrange("(c q e) -> q c e", q=P, e=P)).then_inc(s, 16)
                act.wait_ge(stage_padded, k + 1)
                act.dma_start(stage[0:FULLQ, k, IC - 1, :],
                              a[(IC - 1) * P * P:E - ODD].rearrange("(q e) -> q e", e=P)).then_inc(s, 16)
                act.dma_start(stage[FULLQ:FULLQ + 1, k, IC - 1, 0:ODD],
                              a[E - ODD:E].rearrange("(q e) -> q e", q=1)).then_inc(s, 16)

            def load_weights():
                for to, frm in ((wg[:], Wg), (ws[:], Ws), (w1[:], W1),
                                (w2[:], W2.rearrange("(k p) n -> p k n", p=P)),
                                (w3[:], W3.rearrange("(k p) n -> p k n", p=P)),
                                (bgc[:], bg.rearrange("(p o) -> p o", o=1)),
                                (b1c[:], b1.rearrange("(c p) -> p c", p=P)),
                                (b2c[:], b2.rearrange("(c p) -> p c", p=P)),
                                (b3r[:], b3.rearrange("(o d) -> o d", o=1))):
                    act.dma_start(to, frm, allow_slow_non_contiguous=frm is not W1).then_inc(weights_in, 16)

            def norm_sdev(c):
                s = c % 2
                p, rows, _held = chunk_rows(c)
                act.wait_ge(moments_done, c + 1)
                nc.scalar.activation(sdev[0:p, s, 0:rows], moments[0:p, s, 0:rows, 1], ACT.Sqrt,
                                     bias=eps[0:p, 0:1], scale=1 / SCALE ** 2).then_inc(sdev_ready, 1)

            def norm_scale(c):
                s = c % 2
                p, rows, held = chunk_rows(c)
                at(act, pair_ready, c - 1)
                act.wait_ge(shift_ready, c + 1)
                for r in range(rows):
                    ins = nc.scalar.activation(hval[0:p, s, r], held[0:p, r], ACT.Relu,
                                               bias=shift[0:p, s, r:r + 1], scale=scale[0:p, s, r:r + 1])
                ins.then_inc(scaled, 1)
                act.wait_ge(scaled, c + 1)
                if c - 2 >= TC:
                    act.wait_ge(seg_done, c - 2 - TC + 1)
                elif c >= 2:
                    act.wait_ge(table_in[s], 16 * (c // 2))
                nc.scalar.copy(pair[0:p, s, 0:rows, 0:D], hval[0:p, s, 0:rows]).then_inc(high_ready, 1)

            def cast_stage():
                for k, s in enumerate((src_in, dst_in)):
                    act.wait_ge(s, 48)
                    nc.scalar.copy(stagef[:, k], stage[:, k]).then_inc(stage_cast, 1)

            def take_dst():
                for q in range(TB):
                    n = min(4, IC - 4 * q)
                    act.wait_ge(turned, TB + q + 1)
                    nc.scalar.copy(dst_all[:, 4 * q * P:(4 * q + n) * P], turn_ps[TB + q][:, 0:n * P]
                                   ).then_inc(dst_turned, 1)
                act.wait_ge(dst_turned, TB)
                act.wait_ge(raw_dst_in, 16)
                nc.scalar.copy(dst_all[:, 0:RAWT], raw_dst[:].rearrange("p g j -> p (g j)")).then_inc(dst_ready, 1)

            def take_base():
                act.wait_ge(base_spread, 1)
                nc.scalar.copy(base_all[:], base_ps).then_inc(base_ready, 1)

            act.wait_ge(consts_ready, 1)
            norm_sdev(0)
            for c in range(TC + RAWG):
                if c + 1 < TC + RAWG:
                    norm_sdev(c + 1)
                norm_scale(c)
                if c == 0:
                    load_weights()
                if c == 1:
                    cast_stage()
                if c == TC - 3:
                    take_dst()
                if c == TC - 2:
                    take_base()

            act.wait_ge(weights_in, 16 * 9)

            def dense_block(m, k):
                act.wait_ge(own_turned, k + 1)
                nc.scalar.mul(hownT[:], own_ps, 1 / SCALE).then_inc(hownT_ready, 1)
                act.wait_ge(l1_done, k + 1)
                nc.scalar.activation(h1T[:], l1_ps, ACT.Relu, bias=bgc[:, 0:1]).then_inc(h1_ready, 1)
                for c in range(HC):
                    if c % 2 == 0:
                        act.wait_ge(l2_done, HC // 2 * k + c // 2 + 1)
                    nc.scalar.activation(h2T[:, c], l2_ps[c], ACT.Tanh, bias=b1c[:, c:c + 1]
                                         ).then_inc(h2_ready, 1)
                for c in range(HC):
                    if c % 2 == 0:
                        act.wait_ge(l3_done, HC // 2 * k + c // 2 + 1)
                    nc.scalar.activation(h3T[:, c], l3_ps[c], ACT.Tanh, bias=b2c[:, c:c + 1]
                                         ).then_inc(h3_ready, 1)

            over_blocks(act, dense_block)
            with act.If(is_general(act)):
                again_over_blocks(act, dense_block)

        @block.vector
        def _(dve):
            nc.vector.memset(stage[:, 0, IC - 1, :], 0).then_inc(stage_padded, 1)
            nc.vector.memset(stage[:, 1, IC - 1, :], N).then_inc(stage_padded, 1)
            nc.vector.memset(eps[:], EPS / SCALE ** 2)
            nc.vector.memset(ones32[:], 1.0)
            nc.vector.memset(ones16[:], 1.0).then_inc(consts_ready, 1)

            def norm_stats(c):
                s = c % 2
                p, rows, held = chunk_rows(c)
                if c < TC:
                    dve.wait_ge(x_in[c], 16)
                else:
                    dve.wait_ge(raw_in[c - TC], 16 * GT)
                for r in range(rows):
                    ins = nc.vector.bn_stats(stats[0:p, s, r], held[0:p, r])
                ins.then_inc(stats_done, 1)
                dve.wait_ge(stats_done, c + 1)
                for r in range(rows):
                    ins = nc.vector.bn_aggr(moments[0:p, s, r], stats[0:p, s, r])
                ins.then_inc(moments_done, 1)

            def norm_shift(c):
                s = c % 2
                p, rows, _held = chunk_rows(c)
                dve.wait_ge(sdev_ready, c + 1)
                nc.vector.reciprocal(scale[0:p, s, 0:rows], sdev[0:p, s, 0:rows]).then_inc(scale_done, 1)
                dve.wait_ge(scale_done, c + 1)
                nc.vector.scalar_tensor_tensor(out=shift[0:p, s, 0:rows], in0=moments[0:p, s, 0:rows, 0],
                                               scalar=-1.0, in1=scale[0:p, s, 0:rows],
                                               op0=ALU.mult, op1=ALU.mult).then_inc(shift_ready, 1)

            def norm_low(c):
                s = c % 2
                p, rows, _held = chunk_rows(c)
                dve.wait_ge(high_ready, c + 1)
                nc.vector.tensor_tensor(pair[0:p, s, 0:rows, D:2 * D], hval[0:p, s, 0:rows],
                                        pair[0:p, s, 0:rows, 0:D], ALU.subtract).then_inc(pair_ready, 1)

            def take_idx():
                for q in range(TB):
                    lo = 4 * q * P
                    hi = min(lo + 4 * P, IC * P)
                    dve.wait_ge(turned, q + 1)
                    nc.vector.tensor_copy(idx_all[:, lo:hi], turn_ps[q][:, 0:hi - lo]).then_inc(idx_turned, 1)
                dve.wait_ge(idx_turned, TB)
                dve.wait_ge(raw_idx_in, 16)
                nc.vector.tensor_copy(idx_all[:, 0:RAWT], raw_idx[:].rearrange("p g j -> p (g j)"))
                for g in range(RAWG, RAWG + GPI):
                    nc.vector.tensor_copy(idx_slot[:, (g + AHEAD) % GPI], idx_all[:, g * GT:(g + 1) * GT]
                                          ).then_inc(idx_ready, 1)

            def take_rel():
                dve.wait_ge(base_ready, 1)
                dve.wait_ge(iota_ready, 2)
                nc.vector.tensor_tensor(rel_all[:].rearrange("p (g j) -> p g j", j=GT),
                                        dst_all[:, 0:GROUPS * GT].rearrange("p (g j) -> p g j", j=GT),
                                        base_all[:].unsqueeze(2).to_broadcast([P, GROUPS, GT]),
                                        ALU.subtract).then_inc(rel_ready, 1)
                nc.vector.tensor_tensor(offset[:], base_all[:], origin[:, AHEAD:AHEAD + GROUPS],
                                        ALU.subtract).then_inc(rel_ready, 1)
                dve.wait_ge(rel_ready, 2)
                nc.vector.tensor_scalar(offset_row[:], offset[0:1, :], 0.0, float(SPAN - P), ALU.max, ALU.min
                                        ).then_inc(offset_ready, 1)
                dve.wait_ge(offset_ready, 1)

            def judge():
                nc.vector.tensor_reduce(excess[:, 0:1], rel_all[:], AX.X, ALU.max).then_inc(excess_part, 1)
                nc.vector.tensor_reduce(excess[:, 1:2], rel_all[:], AX.X, ALU.min).then_inc(excess_part, 1)
                nc.vector.tensor_reduce(excess[:, 2:3], offset[:], AX.X, ALU.max).then_inc(excess_part, 1)
                nc.vector.tensor_reduce(excess[:, 3:4], offset[:], AX.X, ALU.min).then_inc(excess_part, 1)
                dve.wait_ge(excess_part, 4)
                nc.vector.tensor_scalar(excess[:, 0:1], excess[:, 0:1], 1.0 - P, None, ALU.add
                                        ).then_inc(excess_part, 1)
                nc.vector.tensor_scalar(excess[:, 2:3], excess[:, 2:3], float(P - SPAN), None, ALU.add
                                        ).then_inc(excess_part, 1)
                nc.vector.tensor_scalar(excess[:, 1::2], excess[:, 1::2], -1.0, None, ALU.mult
                                        ).then_inc(excess_part, 1)
                dve.wait_ge(excess_part, 7)
                nc.vector.tensor_reduce(worst[:], excess[:], AX.X, ALU.max).then_inc(worst_ready, 1)

            def settle():
                dve.wait_ge(excess_turned, 1)
                nc.vector.tensor_reduce(verdict[:], excess_ps, AX.X, ALU.max).then_inc(verdict_ready, 1)
                dve.wait_ge(verdict_ready, 1)
                nc.vector.tensor_scalar(general[:], verdict[:], 0.0, None, ALU.is_gt).then_inc(general_ready, 1)

            def make_onehot(g, b):
                nc.vector.tensor_tensor(onehot[:, b], iota[:, 0:P].unsqueeze(1).to_broadcast([P, GT, P]),
                                        rel_all[:, bass.ds(g * GT, GT)].unsqueeze(2).to_broadcast([P, GT, P]),
                                        ALU.is_equal).then_inc(onehot_ready, 1)

            def add_sums(g, b):
                first = dve.value_load(offset_row[0:1, bass.ds(g, 1)], min_val=0, max_val=SPAN - P)
                at(dve, added, g)
                dve.wait_ge(seg_done, g + 1)
                window = sums[:, :, bass.ds(first, P)]
                nc.vector.tensor_tensor(window, seg_ps[b], window, ALU.add).then_inc(added, 1)

            def fill_idx(g, r):
                nc.vector.tensor_copy(idx_slot[:, r], idx_all[:, bass.ds(g * GT, GT)]).then_inc(idx_ready, 1)

            def move_on(u):
                if not isinstance(u, int) or u > 1:
                    dve.wait_ge(mean_ready, u - 1)
                parts = SPAN // BLK
                for c in range(parts - 1):
                    nc.vector.tensor_copy(sums[:, :, c * BLK:(c + 1) * BLK], sums[:, :, (c + 1) * BLK:(c + 2) * BLK]
                                          ).then_inc(moved, 1)
                    dve.wait_ge(moved, parts * (u - 1) + c + 1)
                nc.vector.memset(sums[:, :, (parts - 1) * BLK:], 0.0).then_inc(moved, 1)
                wait_alone(dve, moved, parts * u, dve_passed)

            def mean(k, total, number):
                nc.vector.tensor_scalar(count[:], number, 1.0, SCALE, ALU.max, ALU.mult).then_inc(count_ready, 1)
                dve.wait_ge(count_ready, k + 1)
                nc.vector.reciprocal(share[:], count[:]).then_inc(share_ready, 1)
                dve.wait_ge(share_ready, k + 1)
                nc.vector.tensor_tensor(meanT[:], total, share[:], ALU.mult).then_inc(mean_ready, 1)

            def residual(k):
                dve.wait_ge(xblk_in, 16 * NT * (k + 1))
                dve.wait_ge(l4_done, k + 1)
                at(dve, out_in, 16 * NT * k)
                nc.vector.tensor_tensor(oblk[:], out_ps, xblk[:], ALU.add).then_inc(oblk_ready, 1)

            def step(u, m):
                for r in range(GPI):
                    g = group(u, r)
                    if g is None:
                        continue
                    static = isinstance(g, int)
                    if not static or g > 0:
                        add_sums(g - 1, (r - 1) % 2)
                    if static and g == 0:
                        make_onehot(0, 0)
                    if not static or g + 1 < GROUPS:
                        make_onehot(g + 1, (r + 1) % 2)
                    if not static or RAWG < g and g + GPI - 1 < GROUPS:
                        fill_idx(g + GPI - 1, (r + GPI - 1) % GPI)
                    if static and g + 1 < RAWG:
                        if g + 3 < RAWG:
                            norm_stats(TC + g + 3)
                        if g + 2 < RAWG:
                            norm_shift(TC + g + 2)
                        norm_low(TC + g + 1)
                    if r == 0:
                        dve.wait_ge(added, g)
                        if m is not None:
                            mean(m, sums[:, 0, 0:BLK], sums[:, 1, 0:BLK])
                        move_on(u)
                if isinstance(u, int) and u == 1:
                    settle()
                if m is not None:
                    residual(m)

            norm_stats(0)
            for c in range(TC):
                norm_stats(c + 1)
                norm_shift(c)
                if c:
                    norm_low(c - 1)
                if c == TC - 3:
                    take_idx()
            norm_stats(TC + 1)
            norm_shift(TC)
            norm_low(TC - 1)
            nc.vector.memset(sums[:], 0.0).then_inc(sums_clear, 1)
            take_rel()
            norm_stats(TC + 2)
            norm_shift(TC + 1)
            norm_low(TC)
            dve.wait_ge(sums_clear, 1)
            judge()
            over_turns(dve, step)
            add_sums(GROUPS - 1, (GROUPS - 1) % 2)
            dve.wait_ge(added, GROUPS)
            mean(BLOCKS - 1, sums[:, 0, 0:BLK], sums[:, 1, 0:BLK])
            residual(BLOCKS - 1)

            with dve.If(is_general(dve)):
                def spread_tile(t, n):
                    nc.vector.tensor_copy(idx_slot[:, 0, 0:1], idx_all[:, bass.ds(t, 1)]).then_inc(gen_idx_ready, 1)
                    nc.vector.tensor_scalar(onehot[:, 0, 0:NT, :].rearrange("p t w -> p (t w)"), iota[:],
                                            dst_all[:, bass.ds(t, 1)], None, ALU.is_equal
                                            ).then_inc(gen_onehot, 1)
                    wait_alone(dve, gen_seg, n, dve_passed)

                def general_block(m, k):
                    over_all_tiles(dve, m, spread_tile)
                    mean(k, gen_sum_ps, gen_count_ps)
                    dve.wait_ge(gen_onehot, (m + 1) * TILES)
                    nc.vector.tensor_scalar(dst_all[:], dst_all[:], float(BLK), None, ALU.subtract
                                            ).then_inc(gen_moved, 1)
                    dve.wait_ge(gen_moved, m + 1)
                    residual(k)

                again_over_blocks(dve, general_block)


_INS = ['x', 'src', 'dst', 'L0_gnn_Wg', 'L0_gnn_Ws', 'L0_gnn_bg', 'L0_gnn_W1', 'L0_gnn_b1',
        'L0_gnn_W2', 'L0_gnn_b2', 'L0_gnn_W3', 'L0_gnn_b3']


def kernel(**inputs):
    import concourse.bacc as _bacc
    from concourse.bass_utils import run_bass_kernel_spmd as _run

    nc = _bacc.Bacc("TRN2", target_bir_lowering=False, num_devices=1)
    arrays, args = {}, []
    for name in _INS:
        a = np.ascontiguousarray(inputs[name])
        arrays[f"in_{name}_dram"] = a
        args.append(nc.dram_tensor(f"in_{name}_dram", a.shape, mybir.dt.from_np(a.dtype), kind="ExternalInput").ap())
    args.append(nc.dram_tensor("out_0_dram", tuple(inputs['x'].shape), F32, kind="ExternalOutput").ap())
    gnn_program(nc, *args)
    r = _run(nc, [arrays], core_ids=[0])
    return r.results[0]["out_0_dram"]
```
